# Optimizing a Trainium2 kernel written in Bass

```python
import numpy as np
import jax
import jax.numpy as jnp

def _softmax(x, axis=-1):
    return jax.nn.softmax(x, axis=axis)

def _gelu(x):
    return jax.nn.gelu(x, approximate=True)

def _silu(x):
    return jax.nn.silu(x)

def _sigmoid(x):
    return jax.nn.sigmoid(x)

def _layernorm(x, axis=-1, eps=1e-05):
    m = jnp.mean(x, axis=axis, keepdims=True)
    v = jnp.var(x, axis=axis, keepdims=True)
    return (x - m) / jnp.sqrt(v + eps)

def _scatter_add(tgt, idx, src, axis=0):
    return tgt.at[idx].add(src)

def _segment_sum(src, seg, n):
    return jax.ops.segment_sum(src, seg, n)
kernel_name = 'mk_adj_resnorm_d1_adj_r2_4c9645'

def setup_inputs(seed: int=0):
    np.random.seed(seed)
    _w = jnp.asarray

    def _rec_inputs():
        import jax
        import jax.numpy as jnp
        _gk = jax.random.key(seed)
        x = -0.000929 + 1 * jax.random.normal(jax.random.fold_in(_gk, 1), (8, 2048, 64), jnp.float32)
        _w = (1.0 + jnp.arange(2048, dtype=jnp.float32)) ** (-0.5)
        _w = _w / _w.mean()
        _pij = jnp.clip(0.0078125 * _w[:, None] * _w[None, :], 0.0, 1.0)
        _a = jax.random.uniform(jax.random.fold_in(_gk, 2), (8, 2048, 2048)) < _pij
        _a = jnp.logical_or(_a, jnp.eye(2048, dtype=bool))
        _af = _a.astype(jnp.float32)
        _af = _af * jax.random.uniform(jax.random.fold_in(_gk, 3), (8, 2048, 2048), jnp.float32, 0.05, 1)
        adj = _af
        return (x, adj)
    x, adj = _rec_inputs()

    def _L0_gnn_setup():
        import jax, jax.numpy as jnp
        import numpy as np
        B, N, C, R = (4, 2048, 64, 16)
        EPS = 1e-12
        key = jax.random.key(seed)
        k_x, k_w, k_u = jax.random.split(key, 3)
        x = jax.random.normal(k_x, (B, N, C), dtype=jnp.float32)
        W = jax.random.uniform(k_w, (B, N, N), dtype=jnp.float32)
        U = 0.01 * jax.random.normal(k_u, (N, R), dtype=jnp.float32)
        w_scale = jnp.asarray(1.0, dtype=jnp.float32)
        return {'x': x, 'W': W, 'U': U, 'w_scale': w_scale}
    _L0_gnn_all = _L0_gnn_setup()
    _L0_gnn_in = {k: v for k, v in _L0_gnn_all.items() if k in ('U', 'w_scale')}
    del _L0_gnn_all
    return {'x': x, 'adj': adj, 'L0_gnn_U': _L0_gnn_in['U'], 'L0_gnn_w_scale': _L0_gnn_in['w_scale']}

def reference(x, adj, L0_gnn_U, L0_gnn_w_scale):
    import jax
    import jax.numpy as jnp

    def _L0_gnn_ref(x, W, U, w_scale):
        import jax, jax.numpy as jnp
        import numpy as np
        B, N, C, R = (4, 2048, 64, 16)
        EPS = 1e-12
        Ws = 0.5 * (W + jnp.swapaxes(W, -1, -2))
        A = jax.nn.sigmoid(U @ U.T)
        K = Ws * A[None, :, :]
        deg = jnp.maximum(K.sum(axis=-1), EPS)
        d = jax.lax.rsqrt(deg)
        K = K * d[:, :, None] * d[:, None, :]
        return w_scale * jnp.einsum('bnm,bmc->bnc', K, x)
    x = _layernorm(x + _L0_gnn_ref(x, adj, L0_gnn_U, L0_gnn_w_scale), axis=-1)
    return x

_drawn_inputs = setup_inputs


def setup_inputs(seed=0):
    import zlib

    import numpy as np

    out = dict(_drawn_inputs(seed))
    spreads = {}
    factors = {'L0_gnn_U': 64.0}
    for name, (base, spread) in spreads.items():
        noise = np.random.default_rng([zlib.crc32(name.encode()), seed]).standard_normal(out[name].shape)
        drawn = base * np.exp(spread * noise) if base else spread * noise
        out[name] = jnp.asarray(drawn.astype(out[name].dtype))
    for name, factor in factors.items():
        out[name] = (out[name] * factor).astype(out[name].dtype)
    return out
```

```python
import concourse.bass as bass
from concourse import mybir
from contextlib import ExitStack


def adjacency_resnorm_kernel(nc: bass.Bass, x: bass.AP, adj: bass.AP, U: bass.AP, w_scale: bass.AP, out: bass.AP):
    f32 = mybir.dt.float32
    ALU = mybir.AluOpType
    ACT = mybir.ActivationFunctionType
    AX = mybir.AxisListType

    P = 128
    B, N, C = x.shape
    R = U.shape[1]
    T = N // P
    W = 4
    NS = T // W
    CH = W * P
    EPS_DEG = 1e-12
    EPS_LN = 1e-5

    UNITS = [(I, S) for S in range(NS) for I in range(S + 1)]
    SUPERS = [sb for I, S in UNITS for sb in ([(I, S), (S, I)] if I < S else [(S, S)])]
    FILLS = [(u, W * I + g, max(W * I + g, W * S), W * (S + 1) - max(W * I + g, W * S))
             for u, (I, S) in enumerate(UNITS) for g in range(W)]
    MIRRORS = [(u, W * S + g, W * I, W if I < S else g, I if I < S else NS)
               for u, (I, S) in enumerate(UNITS) for g in range(W) if I < S or g]
    NF, NM, NSB, NU = len(FILLS), len(MIRRORS), len(SUPERS), len(UNITS)

    def joins_before(m):
        u, j, _, n, slot = MIRRORS[m]
        return W * u + (n if slot == NS else W)

    MIRRORS_AFTER = [[] for _ in range(NF)]
    for m, (u, j, _, _, _) in enumerate(MIRRORS):
        MIRRORS_AFTER[min(W * (u + 1) + j % W, NF - 1)].append(m)
    EARLY, MIDDLE = 4, 9
    PAIRS_BEFORE = [[] for _ in range(NF + 1)]
    for k in range(NSB):
        for h in range(2):
            if k < EARLY:
                at = 0
            elif k < MIDDLE:
                at = 1 + (2 * (k - EARLY) + h) * 11 // (2 * (MIDDLE - EARLY))
            else:
                at = 12 + (2 * (k - MIDDLE) + h) * 12 // (2 * (NSB - MIDDLE))
            PAIRS_BEFORE[at].append((k, h))
    COPY_AFTER_MIRROR, TURN_AFTER_FILL, HALF_AFTER_MIRROR = 17, 27, 20
    SCALE_AFTER_JOIN, MEAN_AFTER_JOIN, SQUARES_AFTER_JOIN, RSTD_AFTER_JOIN = 28, 31, 35, 38
    ROOT_AFTER_MIRROR = 31

    a_at = [P * sum(T - r for r in range(i)) for i in range(T)]

    ctx = ExitStack()
    with ctx:
        def sb(name, shape):
            return ctx.enter_context(nc.sbuf_tensor(name, shape, f32))

        def sem(name):
            return ctx.enter_context(nc.semaphore(name))

        K = sb("K", [P, T, N])
        A = sb("A", [P, P * T * (T + 1) // 2])
        X = sb("X", [P, T, C])
        Z = sb("Z", [P, T, C])
        YT = sb("YT", [P, N])
        H = sb("H", [P, T, C])
        UT = YT
        U4 = K[:, T - 1, :].rearrange("p (t q r) -> p t q r", t=T, q=4)
        SQ = YT[:, 0:T * C].rearrange("p (t c) -> p t c", c=C)
        ident = sb("ident", [P, P])
        u_in = sb("u_in", [P, T, R])
        deg_parts = sb("deg_parts", [P, T, NS + 1])
        deg = sb("deg", [P, T])
        deg_c = sb("deg_c", [P, T])
        deg_root = sb("deg_root", [P, T])
        dinv = sb("dinv", [P, T])
        ws = sb("ws", [P, 1])
        ws_half = sb("ws_half", [P, 1])
        s_out = sb("s_out", [P, T])
        total = sb("total", [P, T])
        mean = sb("mean", [P, T])
        sq_sum = sb("sq_sum", [P, T])
        std = sb("std", [P, T])
        rstd = sb("rstd", [P, T])
        eps_ln = sb("eps_ln", [P, 1])

        Y = ctx.enter_context(nc.psum_tensor("Y", [P, NS, CH], f32))
        FB = ctx.enter_context(nc.psum_tensor("FB", [P, 2, CH], f32))
        MB = ctx.enter_context(nc.psum_tensor("MB", [P, 2, CH], f32))
        YN = Y[:, :, :].rearrange("p s (t c) -> p (s t) c", c=P)

        w_loaded = [sem(f"w_loaded{u}") for u in range(NU)]
        x_loaded = sem("x_loaded")
        u_loaded = sem("u_loaded")
        ws_loaded = sem("ws_loaded")
        const_made = sem("const_made")
        u4_made = sem("u4_made")
        ut_turned = sem("ut_turned")
        ut_made = sem("ut_made")
        logits_made = sem("logits_made")
        a_made = sem("a_made")
        fill_done = sem("fill_done")
        add_done = sem("add_done")
        join_done = sem("join_done")
        mirror_done = sem("mirror_done")
        copy_done = sem("copy_done")
        deg_step = sem("deg_step")
        root_done = sem("root_done")
        ws_made = sem("ws_made")
        z_ready = sem("z_ready")
        s_ready = sem("s_ready")
        super_done = sem("super_done")
        yt_copied = sem("yt_copied")
        y_turned = sem("y_turned")
        half_copied = sem("half_copied")
        h_step = sem("h_step")
        hp_step = sem("hp_step")
        std_done = sem("std_done")
        h_free = sem("h_free")
        DEG_STEPS, H_STEPS, HP_STEPS, CONSTS = 3, 6, 4, 5

        x_v = x.rearrange("b (t p) c -> b p t c", p=P)
        out_v = out.rearrange("b (t p) c -> b p t c", p=P)
        adj_v = adj.rearrange("b (t p) m -> b p t m", p=P)

        def by_node(v, t0=0, t1=T):
            return v[:, t0:t1].unsqueeze(2).broadcast_to([P, t1 - t0, C])

        block = ctx.enter_context(nc.Block())

        @block.sync
        def _(sp):
            sp.dma_start(u_in[:, :, :], U.rearrange("(t p) r -> p t r", p=P)).then_inc(u_loaded, 16)

            def loads(b, first):
                for k, (r, c) in enumerate(SUPERS):
                    if not first:
                        sp.wait_ge(super_done, (b - 1) * NSB + k + 1)
                    elif r == NS - 1 and c == 0:
                        sp.wait_ge(ut_turned, NS)
                    u = UNITS.index((min(r, c), max(r, c)))
                    sp.dma_start(K[:, W * r:W * (r + 1), CH * c:CH * (c + 1)],
                                 adj_v[b, :, W * r:W * (r + 1), CH * c:CH * (c + 1)]).then_inc(w_loaded[u], 16)
                if not first:
                    sp.wait_ge(hp_step, (b - 1) * HP_STEPS + 1)
                sp.dma_start(X[:, :, :], x_v[b]).then_inc(x_loaded, 16)

            def store(b):
                sp.wait_ge(hp_step, b * HP_STEPS + 4)
                sp.dma_start(out_v[b], H[:, :, :]).then_inc(h_free, 16)

            loads(0, True)
            sp.dma_start(ws[:, :], w_scale.broadcast_to([P, 1])).then_inc(ws_loaded, 16)
            with sp.Fori(1, B) as b:
                loads(b, False)
                store(b - 1)
            store(B - 1)
            sp.wait_ge(h_free, 16 * (B + 1))

        @block.gpsimd
        def _(pool):
            pool.memset(ident[:, :], 0.0).then_inc(const_made, 1)
            pool.memset(K[:, T - 1, :], 0.0).then_inc(const_made, 1)
            pool.memset(deg_parts[:, :, :], 0.0).then_inc(const_made, 1)
            pool.memset(eps_ln[:, :], EPS_LN).then_inc(const_made, 1)
            pool.wait_ge(const_made, 4)
            pool.affine_select(out=ident[:, :], in_=ident[:, :], compare_op=ALU.not_equal, fill=1.0, base=0,
                               pattern=[[-1, P]], channel_multiplier=1).then_inc(const_made, 1)
            pool.memset(H[:, :, :], 0.0).then_inc(h_free, 16)

            with pool.Fori(0, B) as b:
                pool.wait_ge(h_step, b * H_STEPS + 2)
                pool.wait_ge(x_loaded, b * 16 + 16)
                pool.tensor_tensor(H[:, :, :], H[:, :, :], X[:, :, :], ALU.add).then_inc(hp_step, 1)
                pool.wait_ge(h_step, b * H_STEPS + 4)
                pool.tensor_tensor(H[:, :, :], H[:, :, :], by_node(mean), ALU.subtract).then_inc(hp_step, 1)
                pool.wait_ge(hp_step, b * HP_STEPS + 2)
                pool.tensor_tensor(SQ, H[:, :, :], H[:, :, :], ALU.mult).then_inc(hp_step, 1)
                pool.wait_ge(h_step, b * H_STEPS + 6)
                pool.tensor_tensor(H[:, :, :], H[:, :, :], by_node(rstd), ALU.mult).then_inc(hp_step, 1)

        @block.scalar
        def _(act):
            for c in range(NS):
                act.wait_ge(ut_turned, c + 1)
                act.activation(UT[:, CH * c:CH * (c + 1)], Y[:, c, :], ACT.Copy).then_inc(ut_made, 1)

            def sigmoids(u):
                act.wait_ge(logits_made, u + 1)
                for g in range(W):
                    _, i, j0, n = FILLS[W * u + g]
                    at = a_at[i] + P * (j0 - i)
                    act.activation(A[:, at:at + P * n], Y[:, g, 0:P * n], ACT.Sigmoid).then_inc(a_made, 1)

            def copy_mirror(b, m):
                _, j, i0, n, part = MIRRORS[m]
                act.wait_ge(mirror_done, b * NM + m + 1)
                act.activation(K[:, j, P * i0:P * (i0 + n)], MB[:, m % 2, 0:P * n], ACT.Copy,
                               accum_out=deg_parts[:, j, part:part + 1]).then_inc(copy_done, 1)

            def copy_products(b):
                act.wait_ge(super_done, b * NSB + NSB)
                for c in range(NS):
                    act.activation(YT[:, CH * c:CH * (c + 1)], Y[:, c, :], ACT.Copy).then_inc(yt_copied, 1)

            def copy_half(b):
                act.wait_ge(y_turned, b + 1)
                act.wait_ge(h_free, b * 16 + 16)
                act.activation(H[:, :, :], YN[:, :, C:2 * C], ACT.Copy).then_inc(half_copied, 1)

            def deviation(b):
                act.wait_ge(h_step, b * H_STEPS + 5)
                act.activation(std[:, :], sq_sum[:, :], ACT.Sqrt, bias=eps_ln[:, 0:1],
                               scale=1.0 / C).then_inc(std_done, 1)

            def batch(b, first):
                if first:
                    sigmoids(0)
                    sigmoids(1)
                for m in range(NM):
                    if first and m % W == 0 and m // W + 2 < NU:
                        sigmoids(m // W + 2)
                    copy_mirror(b, m)
                    if not first and m == COPY_AFTER_MIRROR:
                        copy_products(b - 1)
                    if not first and m == HALF_AFTER_MIRROR:
                        copy_half(b - 1)
                    if not first and m == ROOT_AFTER_MIRROR:
                        deviation(b - 1)
                act.wait_ge(deg_step, b * DEG_STEPS + 2)
                act.activation(deg_root[:, :], deg_c[:, :], ACT.Sqrt).then_inc(root_done, 1)

            act.wait_ge(const_made, CONSTS)
            batch(0, True)
            with act.Fori(1, B) as b:
                batch(b, False)
            copy_products(B - 1)
            copy_half(B - 1)
            deviation(B - 1)

        @block.vector
        def _(dve):
            dve.wait_ge(u_loaded, 16)
            dve.wait_ge(const_made, CONSTS)
            for q in range(4):
                dve.tensor_copy(U4[:, :, q, 0:R], u_in[:, :, :]).then_inc(u4_made, 1)

            def add(b, n):
                _, i, j0, w = FILLS[n]
                row = K[:, i, P * j0:P * (j0 + w)]
                dve.wait_ge(fill_done, b * NF + n + 1)
                dve.tensor_tensor(row, FB[:, n % 2, 0:P * w], row, ALU.add).then_inc(add_done, 1)

            def join(b, n, first):
                u, i, j0, w = FILLS[n]
                row = K[:, i, P * j0:P * (j0 + w)]
                at = a_at[i] + P * (j0 - i)
                S = UNITS[u][1]
                if first:
                    dve.wait_ge(a_made, n + 1)
                dve.wait_ge(add_done, b * NF + n + 1)
                dve.tensor_tensor_reduce(out=row, in0=row, in1=A[:, at:at + P * w], scale=1.0, scalar=0.0,
                                         op0=ALU.mult, op1=ALU.add,
                                         accum_out=deg_parts[:, i, S:S + 1]).then_inc(join_done, 1)

            def scale_products(b):
                dve.wait_ge(half_copied, b + 1)
                dve.tensor_tensor(H[:, :, :], YN[:, :, 0:C], H[:, :, :], ALU.add).then_inc(h_step, 1)
                dve.wait_ge(h_step, b * H_STEPS + 1)
                dve.wait_ge(s_ready, b + 1)
                dve.tensor_tensor(H[:, :, :], H[:, :, :], by_node(s_out), ALU.mult).then_inc(h_step, 1)

            def means(b):
                dve.wait_ge(hp_step, b * HP_STEPS + 1)
                dve.tensor_reduce(total[:, :], H[:, :, :], AX.X, ALU.add).then_inc(h_step, 1)
                dve.wait_ge(h_step, b * H_STEPS + 3)
                dve.tensor_scalar(mean[:, :], total[:, :], 1.0 / C, None, ALU.mult).then_inc(h_step, 1)

            def square_sums(b):
                dve.wait_ge(hp_step, b * HP_STEPS + 3)
                dve.tensor_reduce(sq_sum[:, :], SQ, AX.X, ALU.add).then_inc(h_step, 1)

            def inverse_deviation(b):
                dve.wait_ge(std_done, b + 1)
                dve.reciprocal(rstd[:, :], std[:, :]).then_inc(h_step, 1)

            def degrees(b):
                dve.wait_ge(copy_done, b * NM + NM)
                dve.wait_ge(join_done, b * NF + NF)
                dve.tensor_reduce(deg[:, :], deg_parts[:, :, :], AX.X, ALU.add).then_inc(deg_step, 1)
                dve.wait_ge(deg_step, b * DEG_STEPS + 1)
                dve.tensor_scalar(deg_c[:, :], deg[:, :], 0.5, EPS_DEG, ALU.mult, ALU.max).then_inc(deg_step, 1)
                dve.wait_ge(root_done, b + 1)
                dve.reciprocal(dinv[:, :], deg_root[:, :]).then_inc(deg_step, 1)
                dve.wait_ge(deg_step, b * DEG_STEPS + 3)
                dve.wait_ge(x_loaded, b * 16 + 16)
                for r in range(NS):
                    t0, t1 = W * r, W * (r + 1)
                    dve.tensor_tensor(Z[:, t0:t1, :], X[:, t0:t1, :], by_node(dinv, t0, t1),
                                      ALU.mult).then_inc(z_ready, 1)
                dve.tensor_scalar(s_out[:, :], dinv[:, :], ws_half[:, 0:1], None, ALU.mult).then_inc(s_ready, 1)

            def batch(b, first):
                add(b, 0)
                for n in range(NF):
                    if n + 1 < NF:
                        add(b, n + 1)
                    join(b, n, first)
                    if not first and n == SCALE_AFTER_JOIN:
                        scale_products(b - 1)
                    if not first and n == MEAN_AFTER_JOIN:
                        means(b - 1)
                    if not first and n == SQUARES_AFTER_JOIN:
                        square_sums(b - 1)
                    if not first and n == RSTD_AFTER_JOIN:
                        inverse_deviation(b - 1)
                if first:
                    dve.wait_ge(ws_loaded, 16)
                    dve.tensor_scalar(ws_half[:, :], ws[:, :], 0.5, None, ALU.mult).then_inc(ws_made, 1)
                    dve.wait_ge(ws_made, 1)
                degrees(b)

            batch(0, True)
            with dve.Fori(1, B) as b:
                batch(b, False)
            scale_products(B - 1)
            means(B - 1)
            square_sums(B - 1)
            inverse_deviation(B - 1)

        @block.tensor
        def _(pe):
            pe.wait_ge(const_made, CONSTS)
            pe.wait_ge(u4_made, 4)
            for t in range(T):
                last = pe.transpose(Y[:, t // W, P * (t % W):P * (t % W + 1)], K[:, T - 1, P * t:P * (t + 1)],
                                    ident[:, :])
                if t % W == W - 1:
                    last.then_inc(ut_turned, 1)

            def logits(u):
                if u == 0:
                    pe.wait_ge(ut_made, NS)
                else:
                    pe.wait_ge(a_made, W * u)
                for g in range(W):
                    _, i, j0, n = FILLS[W * u + g]
                    rows = slice(32 * g, 32 * g + R)
                    last = pe.matmul(Y[:, g, 0:P * n], UT[rows, P * i:P * (i + 1)], UT[rows, P * j0:P * (j0 + n)],
                                     start=True, stop=True)
                last.then_inc(logits_made, 1)

            def fill(b, n):
                u, i, j0, w = FILLS[n]
                I, S = UNITS[u]
                if n % W == 0:
                    pe.wait_ge(w_loaded[u], (b + 1) * (32 if I < S else 16))
                if n >= 2 or not isinstance(b, int):
                    pe.wait_ge(add_done, b * NF + n - 1)
                for k in range(w):
                    last = pe.transpose(FB[:, n % 2, P * k:P * (k + 1)], K[:, j0 + k, P * i:P * (i + 1)], ident[:, :])
                last.then_inc(fill_done, 1)

            def mirror(b, m):
                u, j, i0, w, part = MIRRORS[m]
                pe.wait_ge(join_done, b * NF + joins_before(m))
                if m >= 2 or not isinstance(b, int):
                    pe.wait_ge(copy_done, b * NM + m - 1)
                for k in range(w):
                    last = pe.transpose(MB[:, m % 2, P * k:P * (k + 1)], K[:, i0 + k, P * j:P * (j + 1)], ident[:, :])
                last.then_inc(mirror_done, 1)

            def product_pair(b, k, h):
                r, c = SUPERS[k]
                visits = [q for q, (_, cc) in enumerate(SUPERS) if cc == c]
                if h == 0:
                    pe.wait_ge(z_ready, b * NS + r + 1)
                for i in (W * r + 2 * h, W * r + 2 * h + 1):
                    half = slice(C * (i % 2), C * (i % 2) + C)
                    last = pe.matmul(Y[half, c, :], Z[:, i, :], K[:, i, CH * c:CH * (c + 1)],
                                     start=(k == visits[0] and h == 0), stop=(k == visits[-1] and h == 1))
                if h == 1:
                    last.then_inc(super_done, 1)

            def turn_products(b):
                for c in range(NS):
                    pe.wait_ge(yt_copied, b * NS + c + 1)
                    for t in range(W * c, W * (c + 1)):
                        last = pe.transpose(YN[:, t, :], YT[:, P * t:P * (t + 1)], ident[:, :])
                last.then_inc(y_turned, 1)

            def batch(b, first):
                for n in range(NF):
                    if not first:
                        for k, h in PAIRS_BEFORE[n]:
                            product_pair(b - 1, k, h)
                    if first and n % W == 0 and n // W + 1 < NU:
                        logits(n // W + 1)
                    fill(b, n)
                    for m in MIRRORS_AFTER[n]:
                        mirror(b, m)
                    if not first and n == TURN_AFTER_FILL:
                        turn_products(b - 1)

            logits(0)
            batch(0, True)
            with pe.Fori(1, B) as b:
                batch(b, False)
            for k in range(NSB):
                for h in range(2):
                    product_pair(B - 1, k, h)
            turn_products(B - 1)


_INS = ["x", "adj", "L0_gnn_U", "L0_gnn_w_scale"]


def kernel(**inputs):
    import numpy as _np
    import concourse.bacc as _bacc
    from concourse import mybir as _mybir
    from concourse.bass_utils import run_bass_kernel_spmd as _run

    nc = _bacc.Bacc("TRN2", target_bir_lowering=False, num_devices=1, dynamic_dma_scratch_size=1024)
    arrays, args = {}, []
    for name in _INS:
        a = _np.ascontiguousarray(inputs[name])
        if a.ndim == 0:
            a = a.reshape(1)
        arrays[f"in_{name}"] = a
        args.append(nc.dram_tensor(f"in_{name}", a.shape, _mybir.dt.from_np(a.dtype), kind="ExternalInput").ap())
    shape = tuple(inputs["x"].shape)
    args.append(nc.dram_tensor("out_0", shape, _mybir.dt.float32, kind="ExternalOutput").ap())
    adjacency_resnorm_kernel(nc, *args)
    r = _run(nc, [arrays], core_ids=[0])
    return r.results[0]["out_0"]
```

```python
import concourse.bass as bass
from concourse import mybir
from contextlib import ExitStack


def adjacency_resnorm_kernel(nc: bass.Bass, x: bass.AP, adj: bass.AP, U: bass.AP, w_scale: bass.AP, out: bass.AP):
    f32 = mybir.dt.float32
    ALU = mybir.AluOpType
    ACT = mybir.ActivationFunctionType
    AX = mybir.AxisListType

    P = 128
    B, N, C = x.shape
    RANK = U.shape[1]
    Q = 32
    W = P // Q
    T = N // P
    NS = T // W
    CH = W * P
    EPS_DEG = 1e-12
    EPS_LN = 1e-5

    FILLS = [(I, S, (t,)) for I, S in [(0, 1), (0, 2), (1, 2), (0, 3), (1, 3), (2, 3)] for t in range(W)]
    for q, f in enumerate([4, 8, 9, 12, 14, 16, 23, 25, 27, 30, 33, 34]):
        FILLS.insert(f, (q // 3, q // 3, ((0,), (1, 3), (2,))[q % 3]))
    NF = len(FILLS)
    SUPERS = [(1, 0), (0, 1), (0, 0), (2, 0), (0, 2), (1, 1), (2, 1), (1, 2), (2, 2), (0, 3), (3, 0), (3, 1), (1, 3), (3, 3), (3, 2), (2, 3)]
    NSB = len(SUPERS)
    PRODUCTS = [(1, 0), (0, 0), (2, 0), (0, 1), (1, 1), (2, 1), (3, 0), (3, 1)]
    NQ = len(PRODUCTS)
    LAST_PRODUCTS = sorted(PRODUCTS, key=lambda product: product[1])
    Z_ORDER = [1, 0, 2, 3]

    ROWS = [(f, I, S, t, W if I < S else W - t, CH - P if I == S and t == W - 1 else 0)
            for f, (I, S, ts) in enumerate(FILLS) for t in ts]
    NR = len(ROWS)
    PE_TURNS = [f for f, (I, S, _) in enumerate(FILLS) if I == S]
    DVE_TURNS = [f for f, (I, S, _) in enumerate(FILLS) if I < S]
    POOL_JOINS = [n for n, (_, I, S, t, _, _) in enumerate(ROWS) if I < S and t in (1, 3) and (I, S) != (2, 3)]
    DVE_JOINS = [n for n in range(NR) if n not in POOL_JOINS]
    NPT, NVT, NPJ, NDJ = len(PE_TURNS), len(DVE_TURNS), len(POOL_JOINS), len(DVE_JOINS)

    def up_to(items, n):
        return sum(i < n for i in items)

    def rows_needed(I, S, t):
        return 1 + max(n for n, (_, i, s, tt, _, _) in enumerate(ROWS) if (i, s) == (I, S) and (I < S or tt < t))

    MIRRORS = sorted((rows_needed(I, S, t), I, S, t, W if I < S else t)
                     for S in range(NS) for I in range(S + 1) for t in range(W) if I < S or t)
    NM = len(MIRRORS)
    MIRRORS_AT = [[] for _ in range(NF + 1)]
    for m, (rows, _, _, _, _) in enumerate(MIRRORS):
        at = min(ROWS[rows - 1][0] + 1 + 4, NF)
        while at < NF and (MIRRORS_AT[at] and len(MIRRORS_AT[at]) >= 1 or any(MIRRORS_AT[at + 1:])):
            at += 1
        MIRRORS_AT[at].append(m)
    DVE_COPIES = MIRRORS_AT[NF][3:-1:2]
    ACT_COPIES = [m for m in range(NM) if m not in DVE_COPIES]
    NDC, NAC = len(DVE_COPIES), len(ACT_COPIES)
    NFB, NMB, TURN_AHEAD = 3, 3, 0
    AT_ONCE, SOON, SOON_RATE, LAST_PART = 4, 19, 6, 23
    parts = [(q, t) for q in range(NQ) for t in range(W)]
    PARTS_AT = [[] for _ in range(NF + 1)]
    PARTS_AT[0] = parts[:AT_ONCE]
    for n, part in enumerate(parts[AT_ONCE:SOON]):
        PARTS_AT[1 + n // SOON_RATE].append(part)
    start = 1 + -(-(SOON - AT_ONCE) // SOON_RATE)
    for n, part in enumerate(parts[SOON:]):
        PARTS_AT[start + n * (LAST_PART - start) // (len(parts) - SOON)].append(part)
    LOAD_H_AFTER = 15
    STORE_AFTER = 12
    PE_FINAL = 21
    ACT_COPY = 18
    DVE_SCALE = 18
    POOL_ADD_X = 29
    ORDERS = [1, 10, 18, 29]

    LOGITS_AHEAD = 4

    a_at = [P * sum(ROWS[r][4] for r in range(n)) for n in range(NR + 1)]

    ctx = ExitStack()
    with ctx:
        def sb(name, shape):
            return ctx.enter_context(nc.sbuf_tensor(name, shape, f32))

        def sem(name):
            return ctx.enter_context(nc.semaphore(name))

        K = sb("K", [P, NS, NS, W, CH])
        E = sb("E", [P, W, CH])
        sums = sb("sums", [P, 2, CH])
        A = sb("A", [P, a_at[NR]])
        Z = sb("Z", [P, T, C])
        HY = sb("HY", [P, 2, T * C])
        H = HY[:, 0, :].rearrange("p (t c) -> p t c", c=C)
        YT = HY[:, 1, :].rearrange("p (h m) -> p h m", m=CH)
        T1 = YT[:, :, :].rearrange("p h m -> p (h m)").rearrange("p (t c) -> p t c", c=C)
        bf16 = mybir.dt.bfloat16
        UT = HY[:, :, :].bitcast(bf16)
        left, right = (K[:, NS - 1, i, :, :].rearrange("p t m -> p (t m)").rearrange("p (t k r) -> p t k r", t=T, r=RANK)
                       for i in range(2))
        rounded = E[:, 0, 0:T * RANK // 2].bitcast(bf16).rearrange("p (t r) -> p t r", r=RANK)
        rest = E[:, 1, 0:T * RANK].rearrange("p (t r) -> p t r", r=RANK)
        parts_of_u = E[:, 2:4, :].rearrange("p h m -> p (h m)")[:, 0:3 * T * RANK].rearrange("p (t s r) -> p t s r", s=3, r=RANK)
        ident = sb("ident", [P, P])
        u_in = sums[:, 0, 0:T * RANK].rearrange("p (t r) -> p t r", r=RANK)
        deg_parts = sb("deg_parts", [P, T, NS + 1])
        deg = sb("deg", [P, T])
        deg_c = sb("deg_c", [P, T])
        deg_root = sb("deg_root", [P, T])
        dinv = sb("dinv", [P, NS, W])
        ws = sb("ws", [P, 1])
        ws_half = sb("ws_half", [P, 1])
        s_out = sb("s_out", [P, T])
        total = sb("total", [P, T])
        mean = sb("mean", [P, T])
        sq_sum = sb("sq_sum", [P, T])
        std = sb("std", [P, T])
        rstd = sb("rstd", [P, T])
        eps_ln = sb("eps_ln", [P, 1])
        ones = sb("ones", [P, 1])

        Y = ctx.enter_context(nc.psum_tensor("Y", [P, NS // 2, CH], f32))
        FB = ctx.enter_context(nc.psum_tensor("FB", [P, NFB, CH], f32))
        MB = ctx.enter_context(nc.psum_tensor("MB", [P, NMB, CH], f32))

        def in_order(row):
            return row.rearrange("p (a t y) -> p t a y", a=W, t=W)

        def in_blocks(row):
            return row.rearrange("p (t a y) -> p t a y", a=W, t=W)

        def block_of(row, t):
            return row[:, P * t:P * (t + 1)]

        w_loaded = {(r, c): sem(f"w_loaded{r}{c}") for r, c in SUPERS}
        z_loaded = sem("z_loaded")
        h_loaded = sem("h_loaded")
        u_loaded = sem("u_loaded")
        ws_loaded = sem("ws_loaded")
        const_made = sem("const_made")
        split_step = sem("split_step")
        left_made = sem("left_made")
        right_made = sem("right_made")
        ut_turned = sem("ut_turned")
        ut_made = sem("ut_made")
        logits_made = sem("logits_made")
        a_made = sem("a_made")
        e_made = sem("e_made")
        pe_turned = sem("pe_turned")
        dve_turned = sem("dve_turned")
        add_done = sem("add_done")
        dve_joined = sem("dve_joined")
        pool_joined = sem("pool_joined")
        row_summed = sem("row_summed")
        mirror_done = sem("mirror_done")
        copy_done = sem("copy_done")
        dve_copied = sem("dve_copied")
        deg_step = sem("deg_step")
        root_done = sem("root_done")
        ws_made = sem("ws_made")
        z_ready = sem("z_ready")
        scale_step = sem("scale_step")
        product_done = sem("product_done")
        yt_copied = sem("yt_copied")
        y_turned = sem("y_turned")
        h_step = sem("h_step")
        hp_step = sem("hp_step")
        std_done = sem("std_done")
        last_step = sem("last_step")
        last_std = sem("last_std")
        out_stored = sem("out_stored")
        DEG_STEPS, H_STEPS, HP_STEPS, CONSTS, SCALE_STEPS = 3, 6, 4, 5, W * W
        LAST_STEPS, HT = 9, T // 2

        x_v = x.rearrange("b (s a t y) c -> b s a y t c", a=W, t=W, y=Q)
        xn_v = x.rearrange("b (t p) c -> b p t c", p=P)
        out_v = out.rearrange("b (t p) c -> b p t c", p=P)
        adj_v = adj.rearrange("b (s a t y) m -> b s a y t m", a=W, t=W, y=Q)
        adj_g = adj.rearrange("b (s g y) m -> b s y g m", g=W * W, y=Q)

        def by_node(v, t0=0, t1=T):
            return v[:, t0:t1].unsqueeze(2).broadcast_to([P, t1 - t0, C])

        def stack_bank(c):
            return FB[:, c, :] if c < NFB else MB[:, c - NFB, :] if c < NFB + NMB else Y[:, c - NFB - NMB, :]

        def bank_free(engine, b, f):
            if f < NFB:
                if isinstance(b, int):
                    engine.wait_ge(ut_made, 2 * NS)
                    return
                b, f = b - 1, f + NF
            last = max(n for n in range(NR) if ROWS[n][0] == f - NFB)
            if last in DVE_JOINS:
                engine.wait_ge(dve_joined, b * NDJ + up_to(DVE_JOINS, last + 1))
            else:
                engine.wait_ge(add_done, b * NR + last + 1)

        block = ctx.enter_context(nc.Block())

        @block.sync
        def _(sp):
            for s in range(NS):
                for a in range(W):
                    sp.dma_start(u_in[Q * a:Q * (a + 1), W * s:W * (s + 1), :],
                                 U.rearrange("(s a t y) r -> s a y t r", a=W, t=W, y=Q)[s, a]).then_inc(u_loaded, 16)

            def load_super(b, r, c):
                place = K[:, r, c, :, :]
                for a in reversed(range(W)):
                    part = slice(Q * a, Q * (a + 1))
                    if r > c:
                        sp.dma_start(place[part, :, :].rearrange("y t m -> y (t m)").rearrange("y (g m) -> y g m", m=P),
                                     adj_g[b, r, :, :, CH * c + P * a:CH * c + P * (a + 1)]).then_inc(w_loaded[r, c], 16)
                    else:
                        sp.dma_start(place[part, :, :],
                                     adj_v[b, r, a, :, :, CH * c:CH * (c + 1)]).then_inc(w_loaded[r, c], 16)

            def load_z(b):
                for s in range(NS):
                    for a in range(W):
                        sp.dma_start(Z[Q * a:Q * (a + 1), W * s:W * (s + 1), :], x_v[b, s, a]).then_inc(z_loaded, 16)

            def load_h(b):
                sp.dma_start(H[:, :, :], xn_v[b]).then_inc(h_loaded, 16)

            def store(b):
                sp.wait_ge(hp_step, b * HP_STEPS + 4)
                sp.dma_start(out_v[b], H[:, :, :]).then_inc(out_stored, 16)

            def batch(b, stores):
                for k, (row, col) in enumerate(SUPERS):
                    sp.wait_ge(product_done, (b - 1) * NQ + PRODUCTS.index((row, col // 2)) + 1)
                    load_super(b, row, col)
                    if stores and k == STORE_AFTER:
                        store(b - 2)
                    if k == LOAD_H_AFTER:
                        if stores:
                            sp.wait_ge(out_stored, (b - 1) * 16)
                        load_h(b - 1)
                load_z(b)

            for k in range(NSB):
                if SUPERS[k] in ((NS - 1, 0), (NS - 1, 1)):
                    sp.wait_ge(ut_turned, 2 * NS)
                load_super(0, *SUPERS[k])
                if k == 3:
                    load_z(0)
            sp.dma_start(ws[:, :], w_scale.broadcast_to([P, 1])).then_inc(ws_loaded, 16)
            batch(1, False)
            with sp.Fori(2, B) as b:
                batch(b, True)
            store(B - 2)
            sp.wait_ge(out_stored, (B - 1) * 16)
            load_h(B - 1)
            for k in range(2):
                sp.wait_ge(last_step, LAST_STEPS * (k + 1))
                sp.dma_start(out_v[B - 1, :, HT * k:HT * (k + 1), :], H[:, HT * k:HT * (k + 1), :]).then_inc(out_stored, 16)
            sp.wait_ge(out_stored, 16 * (B + 1))

        @block.gpsimd
        def _(pool):
            pool.memset(ident[:, :], 0.0).then_inc(const_made, 1)
            pool.memset(deg_parts[:, :, :], 0.0).then_inc(const_made, 1)
            pool.memset(eps_ln[:, :], EPS_LN).then_inc(const_made, 1)
            pool.memset(ones[:, :], 1.0).then_inc(const_made, 1)
            pool.wait_ge(const_made, CONSTS - 1)
            pool.affine_select(out=ident[:, :], in_=ident[:, :], compare_op=ALU.not_equal, fill=1.0, base=0,
                               pattern=[[-1, P]], channel_multiplier=1).then_inc(const_made, 1)

            def join(b, n, first):
                _, I, S, t, w, at = ROWS[n]
                if first:
                    pool.wait_ge(a_made, n + 1)
                pool.wait_ge(add_done, b * NR + n + 1)
                pool.tensor_tensor(K[:, I, S, t, :], sums[:, up_to(POOL_JOINS, n) % 2, :], A[:, a_at[n]:a_at[n + 1]], ALU.mult).then_inc(pool_joined, 1)

            def add_x(b):
                pool.wait_ge(h_step, b * H_STEPS + 2)
                pool.wait_ge(h_loaded, b * 16 + 16)
                pool.tensor_tensor(H[:, :, :], H[:, :, :], T1, ALU.add).then_inc(hp_step, 1)

            def centre(b):
                pool.wait_ge(h_step, b * H_STEPS + 4)
                pool.tensor_tensor(H[:, :, :], H[:, :, :], by_node(mean), ALU.subtract).then_inc(hp_step, 1)
                pool.wait_ge(hp_step, b * HP_STEPS + 2)
                pool.tensor_tensor(T1, H[:, :, :], H[:, :, :], ALU.mult).then_inc(hp_step, 1)

            def finish(b):
                pool.wait_ge(h_step, b * H_STEPS + 6)
                pool.tensor_tensor(H[:, :, :], H[:, :, :], by_node(rstd), ALU.mult).then_inc(hp_step, 1)

            def batch(b, first):
                for f in range(NF):
                    for n in POOL_JOINS:
                        if ROWS[n][0] == f:
                            join(b, n, first)
                    if not first and f == POOL_ADD_X:
                        add_x(b - 1)
                if not first:
                    centre(b - 1)
                    finish(b - 1)

            batch(0, True)
            with pool.Fori(1, B) as b:
                batch(b, False)

        @block.scalar
        def _(act):
            act.wait_ge(split_step, 6)
            act.activation(right[:, :, 0:6, :].rearrange("p t (k s) r -> p t k (s r)", k=2),
                           parts_of_u.rearrange("p t s r -> p t (s r)").unsqueeze(2).broadcast_to([P, T, 2, 3 * RANK]),
                           ACT.Copy).then_inc(right_made, 1)
            act.activation(right[:, :, 6:8, :], parts_of_u[:, :, 0:2, :], ACT.Copy).then_inc(right_made, 1)
            for c in range(2 * NS):
                act.wait_ge(ut_turned, c + 1)
                act.activation(UT[:, c // NS, CH * (c % NS):CH * (c % NS + 1)], stack_bank(c), ACT.Copy).then_inc(ut_made, 1)

            def sigmoid(n):
                act.wait_ge(logits_made, n + 1)
                act.activation(A[:, a_at[n]:a_at[n + 1]], Y[:, n % 2, 0:P * ROWS[n][4]], ACT.Sigmoid).then_inc(a_made, 1)

            def sum_row(b, n):
                _, I, S, t, _, _ = ROWS[n]
                act.wait_ge(pool_joined, b * NPJ + up_to(POOL_JOINS, n) + 1)
                act.activation(K[:, I, S, t, :], K[:, I, S, t, :], ACT.Copy,
                               accum_out=deg_parts[:, W * I + t, S:S + 1]).then_inc(row_summed, 1)

            def order(b, S):
                act.wait_ge(w_loaded[S, S], (b + 1) * 16 * W)
                if S or not isinstance(b, int):
                    before = (S - 1) % NS
                    rows = 1 + max(n for n in range(NR) if ROWS[n][1:3] == (before, before))
                    act.wait_ge(add_done, (b if S else b - 1) * NR + rows)
                for t in range(W):
                    act.activation(E[:, t, :].rearrange("p (t a y) -> p t a y", a=W, t=W), in_order(K[:, S, S, t, :]),
                                   ACT.Copy).then_inc(e_made, 1)

            def copy_mirror(b, m):
                _, I, S, t, w = MIRRORS[m]
                act.wait_ge(mirror_done, b * NM + m + 1)
                if I < S:
                    act.activation(K[:, S, I, t, :], MB[:, m % NMB, :], ACT.Copy,
                                   accum_out=deg_parts[:, W * S + t, I:I + 1]).then_inc(copy_done, 1)
                else:
                    act.activation(K[:, S, S, t, 0:P * t], MB[:, m % NMB, 0:P * t], ACT.Copy,
                                   accum_out=deg_parts[:, W * S + t, NS:NS + 1]).then_inc(copy_done, 1)

            def copy_products(k):
                act.activation(YT[:, k, :].rearrange("p (a t y) -> p a t y", a=W, t=W),
                               Y[:, k, :].rearrange("p (t a y) -> p a t y", a=W, t=W), ACT.Copy).then_inc(yt_copied, 1)

            def deviation(b):
                act.wait_ge(h_step, b * H_STEPS + 5)
                act.activation(std[:, :], sq_sum[:, :], ACT.Sqrt, bias=eps_ln[:, 0:1],
                               scale=1.0 / C).then_inc(std_done, 1)

            def batch(b, first):
                if first:
                    for n in range(NR):
                        if ROWS[n][0] < LOGITS_AHEAD:
                            sigmoid(n)
                for f in range(NF + 1):
                    for n in range(NR):
                        if first and ROWS[n][0] == f + LOGITS_AHEAD:
                            sigmoid(n)
                    if f in ORDERS:
                        order(b, ORDERS.index(f))
                    for n in POOL_JOINS:
                        if ROWS[n][0] == f - 2 or f == NF and ROWS[n][0] > f - 2:
                            sum_row(b, n)
                    for m in MIRRORS_AT[f]:
                        if m in ACT_COPIES:
                            copy_mirror(b, m)
                    if not first and f == ACT_COPY:
                        act.wait_ge(product_done, (b - 1) * NQ + NQ)
                        for k in range(NS // 2):
                            copy_products(k)
                act.wait_ge(deg_step, b * DEG_STEPS + 2)
                act.activation(deg_root[:, :], deg_c[:, :], ACT.Sqrt).then_inc(root_done, 1)
                if not first:
                    deviation(b - 1)

            act.wait_ge(const_made, CONSTS)
            batch(0, True)
            with act.Fori(1, B) as b:
                batch(b, False)
            for k in range(NS // 2):
                act.wait_ge(product_done, (B - 1) * NQ + NQ // 2 * (k + 1))
                copy_products(k)
            for k in range(2):
                act.wait_ge(last_step, LAST_STEPS * k + 7)
                act.activation(std[:, HT * k:HT * (k + 1)], sq_sum[:, HT * k:HT * (k + 1)], ACT.Sqrt, bias=eps_ln[:, 0:1],
                               scale=1.0 / C).then_inc(last_std, 1)

        @block.vector
        def _(dve):
            dve.wait_ge(u_loaded, 16 * NS * W)
            dve.tensor_copy(rounded, u_in).then_inc(split_step, 1)
            dve.wait_ge(split_step, 1)
            dve.tensor_copy(parts_of_u[:, :, 0, :], rounded).then_inc(split_step, 1)
            dve.wait_ge(split_step, 2)
            dve.tensor_tensor(rest, u_in, parts_of_u[:, :, 0, :], ALU.subtract).then_inc(split_step, 1)
            dve.wait_ge(split_step, 3)
            dve.tensor_copy(rounded, rest).then_inc(split_step, 1)
            dve.wait_ge(split_step, 4)
            dve.tensor_copy(parts_of_u[:, :, 1, :], rounded).then_inc(split_step, 1)
            dve.wait_ge(split_step, 5)
            dve.tensor_tensor(parts_of_u[:, :, 2, :], rest, parts_of_u[:, :, 1, :], ALU.subtract).then_inc(split_step, 1)
            dve.wait_ge(split_step, 6)
            for part, k0, k1 in ((0, 0, 3), (1, 3, 6), (2, 6, 8)):
                dve.tensor_copy(left[:, :, k0:k1, :],
                                parts_of_u[:, :, part, :].unsqueeze(2).broadcast_to([P, T, k1 - k0, RANK])).then_inc(left_made, 1)
            dve.wait_ge(const_made, CONSTS)

            def turn(b, f):
                I, S, (t,) = FILLS[f]
                if t == 0:
                    dve.wait_ge(w_loaded[S, I], (b + 1) * 16 * W)
                bank_free(dve, b, f)
                squares = K[:, S, I, :, :].rearrange("p a (g t x) -> p a g t x", g=W, t=W)[:, :, :, t, :]
                dve.transpose(FB[:, f % NFB, :].rearrange("p (t a y) -> p a t y", a=W, t=W),
                              squares).then_inc(dve_turned, 1)

            def add(b, n):
                f, I, S, t, w, at = ROWS[n]
                bank = FB[:, f % NFB, at:at + P * w]
                if I == S:
                    dve.wait_ge(pe_turned, b * NPT + up_to(PE_TURNS, f) + 1)
                    dve.tensor_tensor(bank, bank, E[:, t, P * t:CH], ALU.add).then_inc(add_done, 1)
                else:
                    if t == 0:
                        dve.wait_ge(w_loaded[I, S], (b + 1) * 16 * W)
                    dve.wait_ge(dve_turned, b * NVT + up_to(DVE_TURNS, f) + 1)
                    if n in POOL_JOINS:
                        q = up_to(POOL_JOINS, n)
                        if q >= 2 or not isinstance(b, int):
                            dve.wait_ge(pool_joined, b * NPJ + q - 1)
                        goal = in_blocks(sums[:, q % 2, :])
                    else:
                        goal = in_blocks(bank)
                    dve.tensor_tensor(goal, in_blocks(bank), in_order(K[:, I, S, t, :]), ALU.add).then_inc(add_done, 1)

            def join(b, n, first):
                f, I, S, t, w, at = ROWS[n]
                if first:
                    dve.wait_ge(a_made, n + 1)
                dve.wait_ge(add_done, b * NR + n + 1)
                dve.tensor_tensor_reduce(out=K[:, I, S, t, CH - P * w:CH], in0=FB[:, f % NFB, at:at + P * w],
                                         in1=A[:, a_at[n]:a_at[n + 1]], scale=1.0, scalar=0.0,
                                         op0=ALU.mult, op1=ALU.add,
                                         accum_out=deg_parts[:, W * I + t, S:S + 1]).then_inc(dve_joined, 1)

            def copy_mirror(b, m):
                _, I, S, t, w = MIRRORS[m]
                dve.wait_ge(mirror_done, b * NM + m + 1)
                part = NS if I == S else I
                dve.tensor_tensor_reduce(out=K[:, S, I, t, 0:P * w], in0=MB[:, m % NMB, 0:P * w],
                                         in1=ones[:, 0:1].broadcast_to([P, P * w]), scale=1.0, scalar=0.0,
                                         op0=ALU.mult, op1=ALU.add,
                                         accum_out=deg_parts[:, W * S + t, part:part + 1]).then_inc(dve_copied, 1)

            def scale_bank(k):
                t0, t1 = 2 * W * k, 2 * W * (k + 1)
                return dve.tensor_tensor(T1[:, t0:t1, :].rearrange("p (h t) c -> p t h c", h=2),
                                         Y[:, k, :].rearrange("p (t h c) -> p t h c", t=W, h=2),
                                         s_out[:, t0:t1].rearrange("p (h t) -> p t h", h=2).unsqueeze(3).broadcast_to([P, W, 2, C]),
                                         ALU.mult)

            def scale_products(b):
                dve.wait_ge(scale_step, b * SCALE_STEPS + SCALE_STEPS)
                for k in range(NS // 2):
                    dve.wait_ge(y_turned, b * (NS // 2) + k + 1)
                    scale_bank(k).then_inc(h_step, 1)

            def means(b):
                dve.wait_ge(hp_step, b * HP_STEPS + 1)
                dve.tensor_reduce(total[:, :], H[:, :, :], AX.X, ALU.add).then_inc(h_step, 1)
                dve.wait_ge(h_step, b * H_STEPS + 3)
                dve.tensor_scalar(mean[:, :], total[:, :], 1.0 / C, None, ALU.mult).then_inc(h_step, 1)

            def square_sums(b):
                dve.wait_ge(hp_step, b * HP_STEPS + 3)
                dve.tensor_reduce(sq_sum[:, :], T1, AX.X, ALU.add).then_inc(h_step, 1)

            def inverse_deviation(b):
                dve.wait_ge(std_done, b + 1)
                dve.reciprocal(rstd[:, :], std[:, :]).then_inc(h_step, 1)

            def finish_half(k):
                t0, t1 = HT * k, HT * (k + 1)
                part_h, part_t = H[:, t0:t1, :], T1[:, t0:t1, :]
                steps = LAST_STEPS * k
                dve.wait_ge(y_turned, (B - 1) * (NS // 2) + k + 1)
                scale_bank(k).then_inc(last_step, 1)
                dve.wait_ge(last_step, steps + 1)
                dve.tensor_tensor(part_h, part_h, part_t, ALU.add).then_inc(last_step, 1)
                dve.wait_ge(last_step, steps + 2)
                dve.tensor_reduce(total[:, t0:t1], part_h, AX.X, ALU.add).then_inc(last_step, 1)
                dve.wait_ge(last_step, steps + 3)
                dve.tensor_scalar(mean[:, t0:t1], total[:, t0:t1], 1.0 / C, None, ALU.mult).then_inc(last_step, 1)
                dve.wait_ge(last_step, steps + 4)
                dve.tensor_tensor(part_h, part_h, by_node(mean, t0, t1), ALU.subtract).then_inc(last_step, 1)
                dve.wait_ge(last_step, steps + 5)
                dve.tensor_tensor(part_t, part_h, part_h, ALU.mult).then_inc(last_step, 1)
                dve.wait_ge(last_step, steps + 6)
                dve.tensor_reduce(sq_sum[:, t0:t1], part_t, AX.X, ALU.add).then_inc(last_step, 1)
                dve.wait_ge(last_std, k + 1)
                dve.reciprocal(rstd[:, t0:t1], std[:, t0:t1]).then_inc(last_step, 1)
                dve.wait_ge(last_step, steps + 8)
                dve.tensor_tensor(part_h, part_h, by_node(rstd, t0, t1), ALU.mult).then_inc(last_step, 1)

            def degrees(b):
                dve.wait_ge(copy_done, b * NAC + NAC)
                if DVE_COPIES:
                    dve.wait_ge(dve_copied, b * NDC + NDC)
                if POOL_JOINS:
                    dve.wait_ge(row_summed, b * NPJ + NPJ)
                dve.wait_ge(dve_joined, b * NDJ + NDJ)
                dve.tensor_reduce(deg[:, :], deg_parts[:, :, :], AX.X, ALU.add).then_inc(deg_step, 1)
                dve.wait_ge(deg_step, b * DEG_STEPS + 1)
                dve.tensor_scalar(deg_c[:, :], deg[:, :], 0.5, EPS_DEG, ALU.mult, ALU.max).then_inc(deg_step, 1)
                dve.wait_ge(root_done, b + 1)
                flat = dinv[:, :, :].rearrange("p s t -> p (s t)")
                dve.reciprocal(flat, deg_root[:, :]).then_inc(deg_step, 1)
                dve.wait_ge(deg_step, b * DEG_STEPS + 3)
                dve.wait_ge(z_loaded, (b + 1) * 16 * NS * W)
                for r in Z_ORDER:
                    t0, t1 = W * r, W * (r + 1)
                    dve.tensor_tensor(Z[:, t0:t1, :], Z[:, t0:t1, :], by_node(flat, t0, t1),
                                      ALU.mult).then_inc(z_ready, 1)
                for a in range(W):
                    for t in range(W):
                        dve.tensor_scalar(s_out[Q * t:Q * (t + 1), a:T:W], dinv[Q * a:Q * (a + 1), :, t],
                                          ws_half[Q * a:Q * (a + 1), 0:1], None, ALU.mult).then_inc(scale_step, 1)

            def batch(b, first):
                for f in range(0, NF, 2):
                    for g in (f, f + 1):
                        if g in DVE_TURNS:
                            turn(b, g)
                    rows = [n for n in range(NR) if ROWS[n][0] in (f, f + 1)]
                    for n in rows:
                        add(b, n)
                    for n in rows:
                        if n in DVE_JOINS:
                            join(b, n, first)
                    if not first and f == DVE_SCALE:
                        scale_products(b - 1)
                for m in DVE_COPIES:
                    copy_mirror(b, m)
                if first:
                    dve.wait_ge(ws_loaded, 16)
                    dve.tensor_scalar(ws_half[:, :], ws[:, :], 0.5, None, ALU.mult).then_inc(ws_made, 1)
                    dve.wait_ge(ws_made, 1)
                degrees(b)
                if not first:
                    means(b - 1)
                    square_sums(b - 1)
                    inverse_deviation(b - 1)

            batch(0, True)
            with dve.Fori(1, B) as b:
                batch(b, False)
            dve.wait_ge(scale_step, B * SCALE_STEPS)
            dve.wait_ge(h_loaded, 16 * B)
            for k in range(2):
                finish_half(k)

        @block.tensor
        def _(pe):
            pe.wait_ge(const_made, CONSTS)
            pe.wait_ge(left_made, 3)
            for c in range(2 * NS):
                if c == NS:
                    pe.wait_ge(right_made, 2)
                stack = (left, right)[c // NS].rearrange("p t k r -> p t (k r)")
                for t in range(W):
                    last = pe.transpose(block_of(stack_bank(c), t), stack[:, W * (c % NS) + t, :], ident[:, :])
                last.then_inc(ut_turned, 1)

            def logits(n):
                if n < 2:
                    pe.wait_ge(ut_made, 2 * NS)
                else:
                    pe.wait_ge(a_made, n - 1)
                _, I, S, t, w, _ = ROWS[n]
                pe.matmul(Y[:, n % 2, 0:P * w], block_of(UT[:, 0, CH * I:CH * (I + 1)], t),
                          UT[:, 1, CH * (S + 1) - P * w:CH * (S + 1)], start=True, stop=True).then_inc(logits_made, 1)

            def turn(b, f):
                _, S, ts = FILLS[f]
                if 0 in ts:
                    pe.wait_ge(e_made, (b * NS + S + 1) * W)
                bank_free(pe, b, f)
                for t in ts:
                    at = CH - P if t == W - 1 else 0
                    for k in range(W - t):
                        last = pe.transpose(block_of(FB[:, f % NFB, at:CH], k), block_of(E[:, t + k, :], t), ident[:, :])
                last.then_inc(pe_turned, 1)

            def mirror(b, m):
                rows, I, S, t, w = MIRRORS[m]
                pe.wait_ge(dve_joined, b * NDJ + up_to(DVE_JOINS, rows))
                if I < S and POOL_JOINS:
                    pe.wait_ge(row_summed, b * NPJ + up_to(POOL_JOINS, rows))
                if m >= NMB or not isinstance(b, int):
                    before, its_batch = (m - NMB, b) if m >= NMB else (m - NMB + NM, b - 1)
                    if before in DVE_COPIES:
                        pe.wait_ge(dve_copied, its_batch * NDC + up_to(DVE_COPIES, before + 1))
                    else:
                        pe.wait_ge(copy_done, its_batch * NAC + up_to(ACT_COPIES, before + 1))
                for k in range(w):
                    last = pe.transpose(block_of(MB[:, m % NMB, :], k), block_of(K[:, I, S, k, :], t), ident[:, :])
                last.then_inc(mirror_done, 1)

            def product_part(b, q, t, products=PRODUCTS):
                r, k = products[q]
                visits = [v for v, (_, kk) in enumerate(products) if kk == k]
                if t == 0:
                    pe.wait_ge(z_ready, b * NS + Z_ORDER.index(r) + 1)
                for h in range(2):
                    last = pe.matmul(Y[C * h:C * (h + 1), k, :], Z[:, W * r + t, :], K[:, r, 2 * k + h, t, :],
                                     start=(q == visits[0] and t == 0), stop=(q == visits[-1] and t == W - 1))
                if t == W - 1:
                    last.then_inc(product_done, 1)

            def turn_products(b, k):
                pe.wait_ge(yt_copied, b * (NS // 2) + k + 1)
                for t in range(W):
                    last = pe.transpose(block_of(Y[:, k, :], t), block_of(YT[:, k, :], t), ident[:, :])
                last.then_inc(y_turned, 1)

            def batch(b, first):
                for f in range(NF + 1):
                    if not first:
                        for q, t in PARTS_AT[f]:
                            product_part(b - 1, q, t)
                    for n in range(NR):
                        if first and ROWS[n][0] == f + LOGITS_AHEAD:
                            logits(n)
                    for g in PE_TURNS:
                        if max(g - TURN_AHEAD, 0) == f:
                            turn(b, g)
                    for m in MIRRORS_AT[f]:
                        mirror(b, m)
                    if not first and f == PE_FINAL:
                        for k in range(NS // 2):
                            turn_products(b - 1, k)

            for n in range(NR):
                if ROWS[n][0] < LOGITS_AHEAD:
                    logits(n)
            batch(0, True)
            with pe.Fori(1, B) as b:
                batch(b, False)
            for q in range(NQ):
                for t in range(W):
                    product_part(B - 1, q, t, LAST_PRODUCTS)
                if q == NQ // 2:
                    turn_products(B - 1, 0)
            turn_products(B - 1, 1)


_INS = ["x", "adj", "L0_gnn_U", "L0_gnn_w_scale"]


def kernel(**inputs):
    import numpy as _np
    import concourse.bacc as _bacc
    from concourse import mybir as _mybir
    from concourse.bass_utils import run_bass_kernel_spmd as _run

    nc = _bacc.Bacc("TRN2", target_bir_lowering=False, num_devices=1, dynamic_dma_scratch_size=1024)
    arrays, args = {}, []
    for name in _INS:
        a = _np.ascontiguousarray(inputs[name])
        if a.ndim == 0:
            a = a.reshape(1)
        arrays[f"in_{name}"] = a
        args.append(nc.dram_tensor(f"in_{name}", a.shape, _mybir.dt.from_np(a.dtype), kind="ExternalInput").ap())
    shape = tuple(inputs["x"].shape)
    args.append(nc.dram_tensor("out_0", shape, _mybir.dt.float32, kind="ExternalOutput").ap())
    adjacency_resnorm_kernel(nc, *args)
    r = _run(nc, [arrays], core_ids=[0])
    return r.results[0]["out_0"]
```

```python
import concourse.bass as bass
from concourse import mybir
from contextlib import ExitStack


def adjacency_resnorm_kernel(nc: bass.Bass, x: bass.AP, adj: bass.AP, U: bass.AP, w_scale: bass.AP, out: bass.AP):
    f32 = mybir.dt.float32
    ALU = mybir.AluOpType
    ACT = mybir.ActivationFunctionType
    AX = mybir.AxisListType

    P = 128
    B, N, C = x.shape
    RANK = U.shape[1]
    Q = 32
    W = P // Q
    T = N // P
    NS = T // W
    CH = W * P
    EPS_DEG = 1e-12
    EPS_LN = 1e-5

    D_ORDER = [1, 0, 2, 3]
    D_FIRST = D_ORDER[0]
    FILLS = [(I, S, (t,)) for I, S in [(0, 1), (0, 2), (1, 2), (0, 3), (1, 3), (2, 3)] for t in range(W)]
    for q, f in enumerate([0, 1, 2, 7, 9, 10, 22, 24, 26, 31, 33, 34]):
        FILLS.insert(f, (D_ORDER[q // 3], D_ORDER[q // 3], ((0,), (1, 3), (2,))[q % 3]))
    NF = len(FILLS)
    SUPERS = [(1, 0), (0, 1), (0, 0), (2, 0), (0, 2), (2, 1), (1, 2), (2, 2),
              (0, 3), (3, 0), (3, 1), (1, 3), (3, 3), (3, 2), (2, 3)]
    PRODUCTS = [(1, 0), (0, 0), (2, 0), (0, 1), (1, 1), (2, 1), (3, 0), (3, 1)]
    NQ = len(PRODUCTS)
    LAST_PRODUCTS = sorted(PRODUCTS, key=lambda product: product[1])
    Z_ORDER = [1, 0, 2, 3]

    ROWS = [(f, I, S, t, W if I < S else W - t, CH - P if I == S and t == W - 1 else 0)
            for f, (I, S, ts) in enumerate(FILLS) for t in ts]
    NR = len(ROWS)
    PE_TURNS = [f for f, (I, S, _) in enumerate(FILLS) if I == S]
    DVE_TURNS = [f for f, (I, S, _) in enumerate(FILLS) if I < S]
    BY_POOL = {(0, 1): (1, 2, 3), (0, 2): (1, 3), (1, 2): (1, 2, 3), (0, 3): (1, 2, 3), (1, 3): (1, 2, 3), (2, 3): (1,)}
    POOL_JOINS = [n for n, (_, I, S, t, _, _) in enumerate(ROWS) if I < S and t in BY_POOL[I, S]]
    DVE_JOINS = [n for n in range(NR) if n not in POOL_JOINS]
    NPT, NVT, NPJ, NDJ = len(PE_TURNS), len(DVE_TURNS), len(POOL_JOINS), len(DVE_JOINS)

    def up_to(items, n):
        return sum(i < n for i in items)

    def rows_needed(I, S, t):
        return 1 + max(n for n, (_, i, s, tt, _, _) in enumerate(ROWS) if (i, s) == (I, S) and (I < S or tt < t))

    MIRRORS = sorted((rows_needed(I, S, t), I, S, t, W if I < S else t)
                     for S in range(NS) for I in range(S + 1) for t in range(W) if I < S or t)
    NM = len(MIRRORS)
    MIRROR_LAG, LAST_FILLS, MIRROR_RATE = 4, 8, 1
    MIRRORS_AT = [[] for _ in range(NF + 1)]
    for m, (rows, _, _, _, _) in enumerate(MIRRORS):
        fill = ROWS[rows - 1][0]
        at = min(fill + 1 + (MIRROR_LAG if fill < NF - LAST_FILLS else 0), NF)
        while at < NF and (len(MIRRORS_AT[at]) >= MIRROR_RATE or any(MIRRORS_AT[at + 1:])):
            at += 1
        MIRRORS_AT[at].append(m)
    DVE_COPIES = MIRRORS_AT[NF][1::2]
    ACT_COPIES = [m for m in range(NM) if m not in DVE_COPIES]
    NDC, NAC = len(DVE_COPIES), len(ACT_COPIES)
    NFB, NMB = 3, 3
    TURN_AHEAD = 1
    AT_ONCE, SOON, SOON_RATE, LAST_PART = 8, 16, 5, 23
    parts = [(q, t) for q in range(NQ) for t in range(W)]
    PARTS_AT = [[] for _ in range(NF + 1)]
    PARTS_AT[0] = parts[:AT_ONCE]
    for n, part in enumerate(parts[AT_ONCE:SOON]):
        PARTS_AT[1 + n // SOON_RATE].append(part)
    start = 1 + -(-(SOON - AT_ONCE) // SOON_RATE)
    for n, part in enumerate(parts[SOON:]):
        PARTS_AT[start + n * (LAST_PART - start) // (len(parts) - SOON)].append(part)
    DVE_SQUARES, ACT_ROOT, DVE_RSTD, POOL_FINISH = 4, 6, 8, 8
    ACT_COPY, PE_FINAL, ACT_Y, POOL_SCALE = 18, 21, 23, 26
    ORDERS = [0, 2, 15, 27]
    LOGITS_AHEAD = 3

    a_at = [P * sum(ROWS[r][4] for r in range(n)) for n in range(NR + 1)]

    ctx = ExitStack()
    with ctx:
        def sb(name, shape):
            return ctx.enter_context(nc.sbuf_tensor(name, shape, f32))

        def sem(name):
            return ctx.enter_context(nc.semaphore(name))

        K = sb("K", [P, NS, NS, W, CH])
        E = sb("E", [P, W, CH])
        sums = sb("sums", [P, 2, CH])
        A = sb("A", [P, a_at[NR]])
        Z = sb("Z", [P, T, C])
        HY = sb("HY", [P, 2, T * C])
        H = HY[:, 0, :].rearrange("p (t c) -> p t c", c=C)
        YT = HY[:, 1, :].rearrange("p (h m) -> p h m", m=CH)
        T1 = YT[:, :, :].rearrange("p h m -> p (h m)").rearrange("p (t c) -> p t c", c=C)
        bf16 = mybir.dt.bfloat16
        UT = HY[:, :, :].bitcast(bf16)
        left, right = (K[:, NS - 1, i, :, :].rearrange("p t m -> p (t m)").rearrange("p (t k r) -> p t k r", t=T, r=RANK)
                       for i in range(2))
        scratch = A[:, a_at[NR] - 4 * CH:a_at[NR]]
        rounded = scratch[:, 0:T * RANK // 2].bitcast(bf16).rearrange("p (t r) -> p t r", r=RANK)
        rest = scratch[:, CH:CH + T * RANK].rearrange("p (t r) -> p t r", r=RANK)
        parts_of_u = scratch[:, 2 * CH:2 * CH + 3 * T * RANK].rearrange("p (t s r) -> p t s r", s=3, r=RANK)
        ident = sb("ident", [P, P])
        u_in = sums[:, 0, 0:T * RANK].rearrange("p (t r) -> p t r", r=RANK)
        deg_parts = sb("deg_parts", [P, T, NS + 1])
        deg = sb("deg", [P, T])
        deg_c = sb("deg_c", [P, T])
        deg_root = sb("deg_root", [P, T])
        dinv = sb("dinv", [P, NS, W])
        ws = sb("ws", [P, 1])
        ws_half = sb("ws_half", [P, 1])
        s_out = sb("s_out", [P, T])
        total = sb("total", [P, T])
        mean = sb("mean", [P, T])
        sq_sum = sb("sq_sum", [P, T])
        std = sb("std", [P, T])
        rstd = sb("rstd", [P, T])
        eps_ln = sb("eps_ln", [P, 1])
        ones = sb("ones", [P, 1])

        Y = ctx.enter_context(nc.psum_tensor("Y", [P, NS // 2, CH], f32))
        FB = ctx.enter_context(nc.psum_tensor("FB", [P, NFB, CH], f32))
        MB = ctx.enter_context(nc.psum_tensor("MB", [P, NMB, CH], f32))

        def in_order(row):
            return row.rearrange("p (a t y) -> p t a y", a=W, t=W)

        def ordered(S):
            return K[:, S, S, :, :] if S == D_FIRST else E

        def in_blocks(row):
            return row.rearrange("p (t a y) -> p t a y", a=W, t=W)

        def block_of(row, t):
            return row[:, P * t:P * (t + 1)]

        w_loaded = {(r, c): sem(f"w_loaded{r}{c}") for r, c in [(D_FIRST, D_FIRST)] + SUPERS}
        z_loaded = sem("z_loaded")
        h_loaded = sem("h_loaded")
        u_loaded = sem("u_loaded")
        ws_loaded = sem("ws_loaded")
        const_made = sem("const_made")
        split_step = sem("split_step")
        left_made = sem("left_made")
        right_made = sem("right_made")
        ut_turned = sem("ut_turned")
        ut_made = sem("ut_made")
        logits_made = sem("logits_made")
        a_made = sem("a_made")
        e_made = sem("e_made")
        pe_turned = sem("pe_turned")
        dve_turned = sem("dve_turned")
        add_done = sem("add_done")
        dve_joined = sem("dve_joined")
        pool_joined = sem("pool_joined")
        row_summed = sem("row_summed")
        mirror_done = sem("mirror_done")
        copy_done = sem("copy_done")
        dve_copied = sem("dve_copied")
        deg_step = sem("deg_step")
        root_done = sem("root_done")
        ws_made = sem("ws_made")
        z_ready = sem("z_ready")
        scale_step = sem("scale_step")
        product_done = sem("product_done")
        yt_copied = sem("yt_copied")
        y_turned = sem("y_turned")
        y_copied = sem("y_copied")
        h_step = sem("h_step")
        hp_step = sem("hp_step")
        std_done = sem("std_done")
        last_step = sem("last_step")
        last_std = sem("last_std")
        out_stored = sem("out_stored")
        DEG_STEPS, H_STEPS, HP_STEPS, CONSTS, SCALE_STEPS = 3, 4, 5, 5, W * W
        LAST_STEPS, HT = 9, T // 2

        x_v = x.rearrange("b (s a t y) c -> b s a y t c", a=W, t=W, y=Q)
        xn_v = x.rearrange("b (t p) c -> b p t c", p=P)
        out_v = out.rearrange("b (t p) c -> b p t c", p=P)
        adj_v = adj.rearrange("b (s a t y) m -> b s a y t m", a=W, t=W, y=Q)
        adj_g = adj.rearrange("b (s g y) m -> b s y g m", g=W * W, y=Q)

        def by_node(v, t0=0, t1=T):
            return v[:, t0:t1].unsqueeze(2).broadcast_to([P, t1 - t0, C])

        def stack_bank(c):
            return FB[:, c, :] if c < NFB else MB[:, c - NFB, :] if c < NFB + NMB else Y[:, c - NFB - NMB, :]

        def is_zero(b):
            return isinstance(b, int) and b == 0

        def bank_free(engine, b, f):
            if f < NFB:
                if is_zero(b):
                    engine.wait_ge(ut_made, 2 * NS)
                    return
                b, f = b - 1, f + NF
            last = max(n for n in range(NR) if ROWS[n][0] == f - NFB)
            if last in DVE_JOINS:
                engine.wait_ge(dve_joined, b * NDJ + up_to(DVE_JOINS, last + 1))
            else:
                engine.wait_ge(add_done, b * NR + last + 1)

        def bank_parts(k):
            return (Y[:, k, :].rearrange("p (t h c) -> p t h c", t=W, h=2),
                    T1[:, 2 * W * k:2 * W * (k + 1), :].rearrange("p (h t) c -> p t h c", h=2))

        def rows_of_diagonal(S):
            return 1 + max(n for n in range(NR) if ROWS[n][1:3] == (S, S))

        block = ctx.enter_context(nc.Block())

        @block.sync
        def _(sp):
            for s in range(NS):
                for a in range(W):
                    sp.dma_start(u_in[Q * a:Q * (a + 1), W * s:W * (s + 1), :],
                                 U.rearrange("(s a t y) r -> s a y t r", a=W, t=W, y=Q)[s, a]).then_inc(u_loaded, 16)

            def load_super(b, r, c):
                place = E if r == c == D_FIRST else K[:, r, c, :, :]
                for a in reversed(range(W)):
                    part = slice(Q * a, Q * (a + 1))
                    if r > c:
                        sp.dma_start(place[part, :, :].rearrange("y t m -> y (t m)").rearrange("y (g m) -> y g m", m=P),
                                     adj_g[b, r, :, :, CH * c + P * a:CH * c + P * (a + 1)]).then_inc(w_loaded[r, c], 16)
                    else:
                        sp.dma_start(place[part, :, :],
                                     adj_v[b, r, a, :, :, CH * c:CH * (c + 1)]).then_inc(w_loaded[r, c], 16)

            def load_z(b):
                for s in range(NS):
                    for a in range(W):
                        sp.dma_start(Z[Q * a:Q * (a + 1), W * s:W * (s + 1), :], x_v[b, s, a]).then_inc(z_loaded, 16)

            def load_h(b):
                sp.dma_start(H[:, :, :], xn_v[b]).then_inc(h_loaded, 16)

            def store(b):
                sp.wait_ge(hp_step, b * HP_STEPS + HP_STEPS)
                sp.dma_start(out_v[b], H[:, :, :]).then_inc(out_stored, 16)

            def load_first(b):
                sp.wait_ge(add_done, (b - 1) * NR + rows_of_diagonal(D_ORDER[-1]))
                load_super(b, D_FIRST, D_FIRST)

            def batch(b, stores):
                load_first(b)
                for row, col in SUPERS:
                    sp.wait_ge(product_done, (b - 1) * NQ + PRODUCTS.index((row, col // 2)) + 1)
                    load_super(b, row, col)
                load_z(b)
                if stores:
                    store(b - 2)
                    sp.wait_ge(out_stored, (b - 1) * 16)
                load_h(b - 1)

            load_super(0, D_FIRST, D_FIRST)
            for k in range(len(SUPERS)):
                if SUPERS[k] in ((NS - 1, 0), (NS - 1, 1)):
                    sp.wait_ge(ut_turned, 2 * NS)
                load_super(0, *SUPERS[k])
                if k == 3:
                    load_z(0)
            sp.dma_start(ws[:, :], w_scale.broadcast_to([P, 1])).then_inc(ws_loaded, 16)
            batch(1, False)
            with sp.Fori(2, B) as b:
                batch(b, True)
            store(B - 2)
            sp.wait_ge(out_stored, (B - 1) * 16)
            load_h(B - 1)
            for k in range(2):
                sp.wait_ge(last_step, LAST_STEPS * (k + 1))
                sp.dma_start(out_v[B - 1, :, HT * k:HT * (k + 1), :], H[:, HT * k:HT * (k + 1), :]).then_inc(out_stored, 16)
            sp.wait_ge(out_stored, 16 * (B + 1))

        @block.gpsimd
        def _(pool):
            pool.memset(ident[:, :], 0.0).then_inc(const_made, 1)
            pool.memset(deg_parts[:, :, :], 0.0).then_inc(const_made, 1)
            pool.memset(eps_ln[:, :], EPS_LN).then_inc(const_made, 1)
            pool.memset(ones[:, :], 1.0).then_inc(const_made, 1)
            pool.wait_ge(const_made, CONSTS - 1)
            pool.affine_select(out=ident[:, :], in_=ident[:, :], compare_op=ALU.not_equal, fill=1.0, base=0,
                               pattern=[[-1, P]], channel_multiplier=1).then_inc(const_made, 1)

            def join(b, n, first):
                _, I, S, t, w, at = ROWS[n]
                if first:
                    pool.wait_ge(a_made, n + 1)
                pool.wait_ge(add_done, b * NR + n + 1)
                pool.tensor_tensor(K[:, I, S, t, :], sums[:, up_to(POOL_JOINS, n) % 2, :], A[:, a_at[n]:a_at[n + 1]], ALU.mult).then_inc(pool_joined, 1)

            def scale_products(b):
                pool.wait_ge(y_copied, (b + 1) * (NS // 2))
                pool.wait_ge(scale_step, b * SCALE_STEPS + SCALE_STEPS)
                pool.tensor_tensor(T1, T1, by_node(s_out), ALU.mult).then_inc(hp_step, 1)

            def add_x(b):
                pool.wait_ge(hp_step, b * HP_STEPS + 1)
                pool.wait_ge(h_loaded, b * 16 + 16)
                pool.tensor_tensor(H[:, :, :], H[:, :, :], T1, ALU.add).then_inc(hp_step, 1)

            def centre(b):
                pool.wait_ge(h_step, b * H_STEPS + 2)
                pool.tensor_tensor(H[:, :, :], H[:, :, :], by_node(mean), ALU.subtract).then_inc(hp_step, 1)
                pool.wait_ge(hp_step, b * HP_STEPS + 3)
                pool.tensor_tensor(T1, H[:, :, :], H[:, :, :], ALU.mult).then_inc(hp_step, 1)

            def finish(b):
                pool.wait_ge(h_step, b * H_STEPS + 4)
                pool.tensor_tensor(H[:, :, :], H[:, :, :], by_node(rstd), ALU.mult).then_inc(hp_step, 1)

            def batch(b, first, third):
                for f in range(NF):
                    for n in POOL_JOINS:
                        if ROWS[n][0] == f:
                            join(b, n, first)
                    if third and f == POOL_FINISH:
                        finish(b - 2)
                    if not first and f == POOL_SCALE:
                        scale_products(b - 1)
                if not first:
                    add_x(b - 1)
                    centre(b - 1)

            batch(0, True, False)
            batch(1, False, False)
            with pool.Fori(2, B) as b:
                batch(b, False, True)
            finish(B - 2)

        @block.scalar
        def _(act):
            act.wait_ge(split_step, 6)
            act.activation(right[:, :, 0:6, :].rearrange("p t (k s) r -> p t k (s r)", k=2),
                           parts_of_u.rearrange("p t s r -> p t (s r)").unsqueeze(2).broadcast_to([P, T, 2, 3 * RANK]),
                           ACT.Copy).then_inc(right_made, 1)
            act.activation(right[:, :, 6:8, :], parts_of_u[:, :, 0:2, :], ACT.Copy).then_inc(right_made, 1)
            for c in range(2 * NS):
                act.wait_ge(ut_turned, c + 1)
                act.activation(UT[:, c // NS, CH * (c % NS):CH * (c % NS + 1)], stack_bank(c), ACT.Copy).then_inc(ut_made, 1)

            def sigmoid(n):
                act.wait_ge(logits_made, n + 1)
                act.activation(A[:, a_at[n]:a_at[n + 1]], Y[:, n % 2, 0:P * ROWS[n][4]], ACT.Sigmoid).then_inc(a_made, 1)

            def sum_row(b, n):
                _, I, S, t, _, _ = ROWS[n]
                act.wait_ge(pool_joined, b * NPJ + up_to(POOL_JOINS, n) + 1)
                act.activation(K[:, I, S, t, :], K[:, I, S, t, :], ACT.Copy,
                               accum_out=deg_parts[:, W * I + t, S:S + 1]).then_inc(row_summed, 1)

            def order(b, S):
                act.wait_ge(w_loaded[S, S], (b + 1) * 16 * W)
                d = D_ORDER.index(S)
                source, goal = (E, K[:, S, S, :, :]) if d == 0 else (K[:, S, S, :, :], E)
                if d == 0 and not is_zero(b):
                    act.wait_ge(product_done, (b - 1) * NQ + PRODUCTS.index((S, S // 2)) + 1)
                if d == 1:
                    act.wait_ge(e_made, (b * NS + 1) * W)
                if d > 1:
                    act.wait_ge(add_done, b * NR + rows_of_diagonal(D_ORDER[d - 1]))
                for t in range(W):
                    act.activation(goal[:, t, :].rearrange("p (t a y) -> p t a y", a=W, t=W), in_order(source[:, t, :]),
                                   ACT.Copy).then_inc(e_made, 1)

            def copy_mirror(b, m):
                _, I, S, t, w = MIRRORS[m]
                act.wait_ge(mirror_done, b * NM + m + 1)
                if I < S:
                    act.activation(K[:, S, I, t, :], MB[:, m % NMB, :], ACT.Copy,
                                   accum_out=deg_parts[:, W * S + t, I:I + 1]).then_inc(copy_done, 1)
                else:
                    act.activation(K[:, S, S, t, 0:P * t], MB[:, m % NMB, 0:P * t], ACT.Copy,
                                   accum_out=deg_parts[:, W * S + t, NS:NS + 1]).then_inc(copy_done, 1)

            def copy_products(k):
                act.activation(YT[:, k, :].rearrange("p (a t y) -> p a t y", a=W, t=W),
                               Y[:, k, :].rearrange("p (t a y) -> p a t y", a=W, t=W), ACT.Copy).then_inc(yt_copied, 1)

            def copy_y(b):
                act.wait_ge(y_turned, (b + 1) * (NS // 2))
                for k in range(NS // 2):
                    y_bank, place = bank_parts(k)
                    act.activation(place, y_bank, ACT.Copy).then_inc(y_copied, 1)

            def deviation(b):
                act.wait_ge(h_step, b * H_STEPS + 3)
                act.activation(std[:, :], sq_sum[:, :], ACT.Sqrt, bias=eps_ln[:, 0:1],
                               scale=1.0 / C).then_inc(std_done, 1)

            def batch(b, first, third):
                if first:
                    for n in range(NR):
                        if ROWS[n][0] < LOGITS_AHEAD:
                            sigmoid(n)
                for f in range(NF + 1):
                    for n in range(NR):
                        if first and ROWS[n][0] == f + LOGITS_AHEAD:
                            sigmoid(n)
                    if f in ORDERS:
                        order(b, D_ORDER[ORDERS.index(f)])
                    if third and f == ACT_ROOT:
                        deviation(b - 2)
                    for n in POOL_JOINS:
                        if ROWS[n][0] == f - 3 or f == NF and ROWS[n][0] > f - 3:
                            sum_row(b, n)
                    for m in MIRRORS_AT[f]:
                        if m in ACT_COPIES:
                            copy_mirror(b, m)
                    if not first and f == ACT_Y:
                        copy_y(b - 1)
                    if not first and f == ACT_COPY:
                        act.wait_ge(product_done, (b - 1) * NQ + NQ)
                        for k in range(NS // 2):
                            copy_products(k)
                act.wait_ge(deg_step, b * DEG_STEPS + 2)
                act.activation(deg_root[:, :], deg_c[:, :], ACT.Sqrt).then_inc(root_done, 1)

            act.wait_ge(const_made, CONSTS)
            batch(0, True, False)
            batch(1, False, False)
            with act.Fori(2, B) as b:
                batch(b, False, True)
            deviation(B - 2)
            for k in range(NS // 2):
                act.wait_ge(product_done, (B - 1) * NQ + NQ // 2 * (k + 1))
                copy_products(k)
            for k in range(2):
                act.wait_ge(last_step, LAST_STEPS * k + 7)
                act.activation(std[:, HT * k:HT * (k + 1)], sq_sum[:, HT * k:HT * (k + 1)], ACT.Sqrt, bias=eps_ln[:, 0:1],
                               scale=1.0 / C).then_inc(last_std, 1)

        @block.vector
        def _(dve):
            dve.wait_ge(u_loaded, 16 * NS * W)
            dve.tensor_copy(rounded, u_in).then_inc(split_step, 1)
            dve.wait_ge(split_step, 1)
            dve.tensor_copy(parts_of_u[:, :, 0, :], rounded).then_inc(split_step, 1)
            dve.wait_ge(split_step, 2)
            dve.tensor_tensor(rest, u_in, parts_of_u[:, :, 0, :], ALU.subtract).then_inc(split_step, 1)
            dve.wait_ge(split_step, 3)
            dve.tensor_copy(rounded, rest).then_inc(split_step, 1)
            dve.wait_ge(split_step, 4)
            dve.tensor_copy(parts_of_u[:, :, 1, :], rounded).then_inc(split_step, 1)
            dve.wait_ge(split_step, 5)
            dve.tensor_tensor(parts_of_u[:, :, 2, :], rest, parts_of_u[:, :, 1, :], ALU.subtract).then_inc(split_step, 1)
            dve.wait_ge(split_step, 6)
            for part, k0, k1 in ((0, 0, 3), (1, 3, 6), (2, 6, 8)):
                dve.tensor_copy(left[:, :, k0:k1, :],
                                parts_of_u[:, :, part, :].unsqueeze(2).broadcast_to([P, T, k1 - k0, RANK])).then_inc(left_made, 1)
            dve.wait_ge(const_made, CONSTS)

            def turn(b, f):
                I, S, (t,) = FILLS[f]
                if t == 0:
                    dve.wait_ge(w_loaded[S, I], (b + 1) * 16 * W)
                bank_free(dve, b, f)
                squares = K[:, S, I, :, :].rearrange("p a (g t x) -> p a g t x", g=W, t=W)[:, :, :, t, :]
                dve.transpose(FB[:, f % NFB, :].rearrange("p (t a y) -> p a t y", a=W, t=W),
                              squares).then_inc(dve_turned, 1)

            def add(b, n):
                f, I, S, t, w, at = ROWS[n]
                bank = FB[:, f % NFB, at:at + P * w]
                if I == S:
                    dve.wait_ge(pe_turned, b * NPT + up_to(PE_TURNS, f) + 1)
                    dve.tensor_tensor(bank, bank, ordered(S)[:, t, P * t:CH], ALU.add).then_inc(add_done, 1)
                else:
                    if t == 0:
                        dve.wait_ge(w_loaded[I, S], (b + 1) * 16 * W)
                    dve.wait_ge(dve_turned, b * NVT + up_to(DVE_TURNS, f) + 1)
                    if n in POOL_JOINS:
                        q = up_to(POOL_JOINS, n)
                        if q >= 2 or not is_zero(b):
                            dve.wait_ge(pool_joined, b * NPJ + q - 1)
                        goal = in_blocks(sums[:, q % 2, :])
                    else:
                        goal = in_blocks(bank)
                    dve.tensor_tensor(goal, in_blocks(bank), in_order(K[:, I, S, t, :]), ALU.add).then_inc(add_done, 1)

            def join(b, n, first):
                f, I, S, t, w, at = ROWS[n]
                if first:
                    dve.wait_ge(a_made, n + 1)
                dve.wait_ge(add_done, b * NR + n + 1)
                dve.tensor_tensor_reduce(out=K[:, I, S, t, CH - P * w:CH], in0=FB[:, f % NFB, at:at + P * w],
                                         in1=A[:, a_at[n]:a_at[n + 1]], scale=1.0, scalar=0.0,
                                         op0=ALU.mult, op1=ALU.add,
                                         accum_out=deg_parts[:, W * I + t, S:S + 1]).then_inc(dve_joined, 1)

            def copy_mirror(b, m):
                _, I, S, t, w = MIRRORS[m]
                dve.wait_ge(mirror_done, b * NM + m + 1)
                part = NS if I == S else I
                dve.tensor_tensor_reduce(out=K[:, S, I, t, 0:P * w], in0=MB[:, m % NMB, 0:P * w],
                                         in1=ones[:, 0:1].broadcast_to([P, P * w]), scale=1.0, scalar=0.0,
                                         op0=ALU.mult, op1=ALU.add,
                                         accum_out=deg_parts[:, W * S + t, part:part + 1]).then_inc(dve_copied, 1)

            def means(b):
                dve.wait_ge(hp_step, b * HP_STEPS + 2)
                dve.tensor_reduce(total[:, :], H[:, :, :], AX.X, ALU.add).then_inc(h_step, 1)
                dve.wait_ge(h_step, b * H_STEPS + 1)
                dve.tensor_scalar(mean[:, :], total[:, :], 1.0 / C, None, ALU.mult).then_inc(h_step, 1)

            def square_sums(b):
                dve.wait_ge(hp_step, b * HP_STEPS + 4)
                dve.tensor_reduce(sq_sum[:, :], T1, AX.X, ALU.add).then_inc(h_step, 1)

            def inverse_deviation(b):
                dve.wait_ge(std_done, b + 1)
                dve.reciprocal(rstd[:, :], std[:, :]).then_inc(h_step, 1)

            def finish_half(k):
                t0, t1 = HT * k, HT * (k + 1)
                part_h, part_t = H[:, t0:t1, :], T1[:, t0:t1, :]
                steps = LAST_STEPS * k
                dve.wait_ge(y_turned, (B - 1) * (NS // 2) + k + 1)
                y_bank, place = bank_parts(k)
                by_block = s_out[:, t0:t1].rearrange("p (h t) -> p t h", h=2).unsqueeze(3).broadcast_to([P, W, 2, C])
                dve.tensor_tensor(place, y_bank, by_block, ALU.mult).then_inc(last_step, 1)
                dve.wait_ge(last_step, steps + 1)
                dve.tensor_tensor(part_h, part_h, part_t, ALU.add).then_inc(last_step, 1)
                dve.wait_ge(last_step, steps + 2)
                dve.tensor_reduce(total[:, t0:t1], part_h, AX.X, ALU.add).then_inc(last_step, 1)
                dve.wait_ge(last_step, steps + 3)
                dve.tensor_scalar(mean[:, t0:t1], total[:, t0:t1], 1.0 / C, None, ALU.mult).then_inc(last_step, 1)
                dve.wait_ge(last_step, steps + 4)
                dve.tensor_tensor(part_h, part_h, by_node(mean, t0, t1), ALU.subtract).then_inc(last_step, 1)
                dve.wait_ge(last_step, steps + 5)
                dve.tensor_tensor(part_t, part_h, part_h, ALU.mult).then_inc(last_step, 1)
                dve.wait_ge(last_step, steps + 6)
                dve.tensor_reduce(sq_sum[:, t0:t1], part_t, AX.X, ALU.add).then_inc(last_step, 1)
                dve.wait_ge(last_std, k + 1)
                dve.reciprocal(rstd[:, t0:t1], std[:, t0:t1]).then_inc(last_step, 1)
                dve.wait_ge(last_step, steps + 8)
                dve.tensor_tensor(part_h, part_h, by_node(rstd, t0, t1), ALU.mult).then_inc(last_step, 1)

            def degrees(b):
                dve.wait_ge(copy_done, b * NAC + NAC)
                if DVE_COPIES:
                    dve.wait_ge(dve_copied, b * NDC + NDC)
                if POOL_JOINS:
                    dve.wait_ge(row_summed, b * NPJ + NPJ)
                dve.wait_ge(dve_joined, b * NDJ + NDJ)
                dve.tensor_reduce(deg[:, :], deg_parts[:, :, :], AX.X, ALU.add).then_inc(deg_step, 1)
                dve.wait_ge(deg_step, b * DEG_STEPS + 1)
                dve.tensor_scalar(deg_c[:, :], deg[:, :], 0.5, EPS_DEG, ALU.mult, ALU.max).then_inc(deg_step, 1)
                dve.wait_ge(root_done, b + 1)
                flat = dinv[:, :, :].rearrange("p s t -> p (s t)")
                dve.reciprocal(flat, deg_root[:, :]).then_inc(deg_step, 1)
                dve.wait_ge(deg_step, b * DEG_STEPS + 3)
                dve.wait_ge(z_loaded, (b + 1) * 16 * NS * W)
                for r in Z_ORDER:
                    t0, t1 = W * r, W * (r + 1)
                    dve.tensor_tensor(Z[:, t0:t1, :], Z[:, t0:t1, :], by_node(flat, t0, t1),
                                      ALU.mult).then_inc(z_ready, 1)
                for a in range(W):
                    for t in range(W):
                        dve.tensor_scalar(s_out[Q * t:Q * (t + 1), a:T:W], dinv[Q * a:Q * (a + 1), :, t],
                                          ws_half[Q * a:Q * (a + 1), 0:1], None, ALU.mult).then_inc(scale_step, 1)

            def batch(b, first, third):
                for f in range(0, NF, 2):
                    for g in (f, f + 1):
                        if g in DVE_TURNS:
                            turn(b, g)
                    if third and f == DVE_SQUARES:
                        square_sums(b - 2)
                    if third and f == DVE_RSTD:
                        inverse_deviation(b - 2)
                    rows = [n for n in range(NR) if ROWS[n][0] in (f, f + 1)]
                    for n in rows:
                        add(b, n)
                    for n in rows:
                        if n in DVE_JOINS:
                            join(b, n, first)
                for m in DVE_COPIES:
                    copy_mirror(b, m)
                if first:
                    dve.wait_ge(ws_loaded, 16)
                    dve.tensor_scalar(ws_half[:, :], ws[:, :], 0.5, None, ALU.mult).then_inc(ws_made, 1)
                    dve.wait_ge(ws_made, 1)
                degrees(b)
                if not first:
                    means(b - 1)

            batch(0, True, False)
            batch(1, False, False)
            with dve.Fori(2, B) as b:
                batch(b, False, True)
            square_sums(B - 2)
            inverse_deviation(B - 2)
            dve.wait_ge(scale_step, B * SCALE_STEPS)
            dve.wait_ge(h_loaded, 16 * B)
            for k in range(2):
                finish_half(k)

        @block.tensor
        def _(pe):
            pe.wait_ge(const_made, CONSTS)
            pe.wait_ge(left_made, 3)
            for c in range(2 * NS):
                if c == NS:
                    pe.wait_ge(right_made, 2)
                stack = (left, right)[c // NS].rearrange("p t k r -> p t (k r)")
                for t in range(W):
                    last = pe.transpose(block_of(stack_bank(c), t), stack[:, W * (c % NS) + t, :], ident[:, :])
                last.then_inc(ut_turned, 1)

            def logits(n):
                if n < 2:
                    pe.wait_ge(ut_made, 2 * NS)
                else:
                    pe.wait_ge(a_made, n - 1)
                _, I, S, t, w, _ = ROWS[n]
                columns = slice(CH * (S + 1) - P * w, CH * (S + 1))
                pe.matmul(Y[:, n % 2, 0:P * w], block_of(UT[:, 0, CH * I:CH * (I + 1)], t), UT[:, 1, columns],
                          start=True, stop=False)
                low = slice(2 * RANK, 3 * RANK)
                pe.matmul(Y[:, n % 2, 0:P * w], block_of(UT[low, 1, CH * I:CH * (I + 1)], t), UT[low, 1, columns],
                          start=False, stop=True).then_inc(logits_made, 1)

            def turn(b, f):
                _, S, ts = FILLS[f]
                if 0 in ts:
                    pe.wait_ge(e_made, (b * NS + D_ORDER.index(S) + 1) * W)
                bank_free(pe, b, f)
                for t in ts:
                    at = CH - P if t == W - 1 else 0
                    for k in range(W - t):
                        last = pe.transpose(block_of(FB[:, f % NFB, at:CH], k), block_of(ordered(S)[:, t + k, :], t), ident[:, :])
                last.then_inc(pe_turned, 1)

            def mirror(b, m):
                rows, I, S, t, w = MIRRORS[m]
                pe.wait_ge(dve_joined, b * NDJ + up_to(DVE_JOINS, rows))
                if I < S and POOL_JOINS:
                    pe.wait_ge(row_summed, b * NPJ + up_to(POOL_JOINS, rows))
                if m >= NMB or not is_zero(b):
                    before, its_batch = (m - NMB, b) if m >= NMB else (m - NMB + NM, b - 1)
                    if before in DVE_COPIES:
                        pe.wait_ge(dve_copied, its_batch * NDC + up_to(DVE_COPIES, before + 1))
                    else:
                        pe.wait_ge(copy_done, its_batch * NAC + up_to(ACT_COPIES, before + 1))
                for k in range(w):
                    last = pe.transpose(block_of(MB[:, m % NMB, :], k), block_of(K[:, I, S, k, :], t), ident[:, :])
                last.then_inc(mirror_done, 1)

            def product_part(b, q, t, products=PRODUCTS):
                r, k = products[q]
                visits = [v for v, (_, kk) in enumerate(products) if kk == k]
                if t == 0:
                    pe.wait_ge(z_ready, b * NS + Z_ORDER.index(r) + 1)
                for h in range(2):
                    last = pe.matmul(Y[C * h:C * (h + 1), k, :], Z[:, W * r + t, :], K[:, r, 2 * k + h, t, :],
                                     start=(q == visits[0] and t == 0), stop=(q == visits[-1] and t == W - 1))
                if t == W - 1:
                    last.then_inc(product_done, 1)

            def turn_products(b, k):
                pe.wait_ge(yt_copied, b * (NS // 2) + k + 1)
                for t in range(W):
                    last = pe.transpose(block_of(Y[:, k, :], t), block_of(YT[:, k, :], t), ident[:, :])
                last.then_inc(y_turned, 1)

            def batch(b, first):
                for f in range(NF + 1):
                    if not first:
                        for q, t in PARTS_AT[f]:
                            product_part(b - 1, q, t)
                    for n in range(NR):
                        if first and ROWS[n][0] == f + LOGITS_AHEAD:
                            logits(n)
                    for g in PE_TURNS:
                        if max(g - TURN_AHEAD, 0) == f:
                            turn(b, g)
                    for m in MIRRORS_AT[f]:
                        mirror(b, m)
                    if not first and f == PE_FINAL:
                        for k in range(NS // 2):
                            turn_products(b - 1, k)

            for n in range(NR):
                if ROWS[n][0] < LOGITS_AHEAD:
                    logits(n)
            batch(0, True)
            with pe.Fori(1, B) as b:
                batch(b, False)
            for q in range(NQ):
                for t in range(W):
                    product_part(B - 1, q, t, LAST_PRODUCTS)
                if q == NQ // 2:
                    turn_products(B - 1, 0)
            turn_products(B - 1, 1)


_INS = ["x", "adj", "L0_gnn_U", "L0_gnn_w_scale"]


def kernel(**inputs):
    import numpy as _np
    import concourse.bacc as _bacc
    from concourse import mybir as _mybir
    from concourse.bass_utils import run_bass_kernel_spmd as _run

    nc = _bacc.Bacc("TRN2", target_bir_lowering=False, num_devices=1, dynamic_dma_scratch_size=1024)
    arrays, args = {}, []
    for name in _INS:
        a = _np.ascontiguousarray(inputs[name])
        if a.ndim == 0:
            a = a.reshape(1)
        arrays[f"in_{name}"] = a
        args.append(nc.dram_tensor(f"in_{name}", a.shape, _mybir.dt.from_np(a.dtype), kind="ExternalInput").ap())
    shape = tuple(inputs["x"].shape)
    args.append(nc.dram_tensor("out_0", shape, _mybir.dt.float32, kind="ExternalOutput").ap())
    adjacency_resnorm_kernel(nc, *args)
    r = _run(nc, [arrays], core_ids=[0])
    return r.results[0]["out_0"]
```
